# Optimizing a Trainium2 kernel written in Bass

```python
import numpy as np
import jax
import jax.numpy as jnp

def _softmax(x, axis=-1):
    return jax.nn.softmax(x, axis=axis)
def _gelu(x):
    return jax.nn.gelu(x, approximate=True)
def _silu(x):
    return jax.nn.silu(x)
def _sigmoid(x):
    return jax.nn.sigmoid(x)
def _layernorm(x, axis=-1, eps=1e-5):
    m = jnp.mean(x, axis=axis, keepdims=True)
    v = jnp.var(x, axis=axis, keepdims=True)
    return (x - m) / jnp.sqrt(v + eps)
def _scatter_add(tgt, idx, src, axis=0):
    return tgt.at[idx].add(src)
def _segment_sum(src, seg, n):
    return jax.ops.segment_sum(src, seg, n)

kernel_name = 'mk_conv_seq_d2_conv_nchw512_5059f5'

def setup_inputs(seed: int = 0):
    np.random.seed(seed)
    _w = jnp.asarray
    def _rec_inputs():
        import jax
        import jax.numpy as jnp
        _gk = jax.random.key(seed)
        x = -7.109e-05 + 0.9999 * jax.random.normal(jax.random.fold_in(_gk, 1), (8, 512, 128, 128), jnp.float32)
        return x
    x = _rec_inputs()
    def _L0_conv_setup():
        import jax, jax.numpy as jnp
        import numpy as np
        B, CH, H, W = (8, 512, 128, 128)
        K, N = (8, 2)
        KM_ITERS, EM_ITERS = (10, 10)
        EPS = 1e-06

        def _kmeans_labels(xs):
            c = xs.shape[0]
            init_idx = jnp.round(jnp.linspace(0.0, c - 1.0, K)).astype(jnp.int32)
            cent = xs[init_idx]
            x2 = (xs ** 2).sum(1, keepdims=True)
            for _ in range(KM_ITERS):
                d = x2 - 2.0 * (xs @ cent.T) + (cent ** 2).sum(1)[None, :]
                labels = jnp.argmin(d, axis=1)
                oh = jax.nn.one_hot(labels, K, dtype=xs.dtype)
                cnt = oh.sum(0)
                new_cent = oh.T @ xs / jnp.maximum(cnt, 1.0)[:, None]
                cent = jnp.where((cnt > 0.0)[:, None], new_cent, cent)
            d = x2 - 2.0 * (xs @ cent.T) + (cent ** 2).sum(1)[None, :]
            return jnp.argmin(d, axis=1)

        def _gmm_fit(data):
            b, P, k = data.shape
            pick = jnp.round(jnp.linspace(0.0, P - 1.0, N)).astype(jnp.int32)
            mu = data[:, pick, :]
            var = jnp.broadcast_to(data.var(axis=1, keepdims=True) + EPS, mu.shape)
            wts = jnp.full((b, N), 1.0 / N, dtype=data.dtype)
            log2pi = jnp.log(2.0 * jnp.pi).astype(data.dtype)
            for _ in range(EM_ITERS):
                diff2 = ((data[:, :, None, :] - mu[:, None, :, :]) ** 2 / var[:, None, :, :]).sum(-1)
                logdet = jnp.log(var).sum(-1)
                logp = -0.5 * (diff2 + logdet[:, None, :] + k * log2pi) + jnp.log(wts)[:, None, :]
                resp = jax.nn.softmax(logp, axis=2)
                Nk = resp.sum(1)
                mu = jnp.einsum('bpn,bpk->bnk', resp, data) / Nk[..., None]
                ex2 = jnp.einsum('bpn,bpk->bnk', resp, data ** 2) / Nk[..., None]
                var = jnp.maximum(ex2 - mu ** 2 + EPS, EPS)
                wts = Nk / P
            return (mu, var)

        def _bilinear_up_x2(x):
            b, c, h, w = x.shape

            def coords(n_in, n_out):
                s = jnp.linspace(0.0, n_in - 1.0, n_out)
                i0 = jnp.floor(s).astype(jnp.int32)
                i1 = jnp.minimum(i0 + 1, n_in - 1)
                return (i0, i1, (s - i0).astype(x.dtype))
            y0, y1, fy = coords(h, 2 * h)
            x0, x1, fx = coords(w, 2 * w)
            rows = x[:, :, y0, :] * (1.0 - fy)[None, None, :, None] + x[:, :, y1, :] * fy[None, None, :, None]
            return rows[:, :, :, x0] * (1.0 - fx) + rows[:, :, :, x1] * fx

        def _forward(sx, w_down, w_conv, w_up):
            c2 = sx.shape[1] // 2
            x = jax.lax.conv_general_dilated(sx, w_down, window_strides=(2, 2), padding=((1, 1), (1, 1)), feature_group_count=c2, dimension_numbers=('NCHW', 'OIHW', 'NCHW'))
            b, c, h, w = x.shape
            xx = jax.lax.stop_gradient(x[0].reshape(c, h * w))
            mn = xx.min(axis=1, keepdims=True)
            mx = xx.max(axis=1, keepdims=True)
            xs = (xx - mn) / jnp.maximum(mx - mn, 1e-12)
            labels = _kmeans_labels(xs)
            oh = jax.nn.one_hot(labels, K, dtype=xx.dtype)
            cnt = oh.sum(0)
            cl_mean = oh.T @ xx / jnp.maximum(cnt, 1.0)[:, None]
            v22 = cl_mean.std(axis=1)
            order = jnp.argsort(v22)
            inv = jnp.argsort(order)
            slabel = inv[labels]
            soh = jax.nn.one_hot(slabel, K, dtype=x.dtype)
            scnt = soh.sum(0)
            v5 = jnp.einsum('bchw,ck->bkhw', x, soh / jnp.maximum(scnt, 1.0)[None, :])
            wa = jax.lax.stop_gradient(v5.reshape(b, K, h * w).transpose(0, 2, 1))
            mu, var = _gmm_fit(wa)
            v6 = mu.transpose(0, 2, 1)
            v66 = var.transpose(0, 2, 1)
            box = jnp.take_along_axis(v6, jnp.argsort(v66, axis=2), axis=2)
            y = jax.nn.sigmoid(jnp.einsum('bkn,kn->bk', box, w_conv))
            gate = y[:, slabel]
            pre_up = gate[:, :, None, None] * x + x
            up = jnp.repeat(pre_up, 2, axis=1) * w_up[None, :, None, None]
            return _bilinear_up_x2(up) + sx
        key = jax.random.key(seed)
        k1, k2, k3, k4 = jax.random.split(key, 4)
        sx = jax.random.normal(k1, (B, CH, H, W), dtype=jnp.float32)
        w_down = jax.random.normal(k2, (CH // 2, 2, 3, 3), dtype=jnp.float32) * 0.1
        w_conv = jax.random.normal(k3, (K, N), dtype=jnp.float32) * 0.5
        w_up = jax.random.normal(k4, (CH,), dtype=jnp.float32) * 0.1
        return {'sx': sx, 'w_down': w_down, 'w_conv': w_conv, 'w_up': w_up}
    _L0_conv_all = _L0_conv_setup()
    _L0_conv_in = {k: v for k, v in _L0_conv_all.items() if k in ('w_down', 'w_conv', 'w_up', )}
    del _L0_conv_all

    def _L1_conv_setup():
        import jax, jax.numpy as jnp
        import numpy as np
        UP = 2
        DOWN = 2
        NEG_SLOPE = 0.2
        MARGIN = 10
        FLRELU_SCALE = np.float32(2.0 ** 0.5)
        UP_PAD = ((10 + 1) // 2 + UP - 1, 10 // 2)
        DOWN_PAD = ((10 + 1) // 2, 10 // 2)
        _FILT = np.array([0.0, 0.00398, -0.01884, -0.05155, 0.12443, 0.44197, 0.44197, 0.12443, -0.05155, -0.01884, 0.00398, 0.0], dtype=np.float32)
        _FILT = _FILT / _FILT.sum()

        def _fir1d(x, k, up, down, pad0, pad1, axis):
            N, C, H, W = x.shape
            xr = x.reshape(N * C, 1, H, W)
            K = k.shape[0]
            kf = k[::-1].astype(x.dtype)
            if axis == 3:
                w = kf.reshape(1, 1, 1, K)
                lhs_dil = (1, up)
                strides = (1, down)
                padding = ((0, 0), (pad0, pad1 + up - 1))
            else:
                w = kf.reshape(1, 1, K, 1)
                lhs_dil = (up, 1)
                strides = (down, 1)
                padding = ((pad0, pad1 + up - 1), (0, 0))
            y = jax.lax.conv_general_dilated(xr, w, window_strides=strides, padding=padding, lhs_dilation=lhs_dil, dimension_numbers=('NCHW', 'OIHW', 'NCHW'))
            return y.reshape(N, C, y.shape[2], y.shape[3])

        def _sep_upfirdn(x, k, up, down, pad):
            x = _fir1d(x, k, up, down, pad[0], pad[1], axis=3)
            x = _fir1d(x, k, up, down, pad[0], pad[1], axis=2)
            return x
        key = jax.random.key(seed)
        k_in = jax.random.fold_in(key, 0)
        return {'input': jax.random.normal(k_in, (8, 512, 64, 64), dtype=jnp.float32), 'bias': jnp.zeros((512,), dtype=jnp.float32), 'up_filter': jnp.asarray(_FILT), 'down_filter': jnp.asarray(_FILT)}
    _L1_conv_all = _L1_conv_setup()
    _L1_conv_in = {k: v for k, v in _L1_conv_all.items() if k in ('bias', 'up_filter', 'down_filter', )}
    del _L1_conv_all

    return {
        "x": x,
        "L0_conv_w_down": _L0_conv_in["w_down"],
        "L0_conv_w_conv": _L0_conv_in["w_conv"],
        "L0_conv_w_up": _L0_conv_in["w_up"],
        "L1_conv_bias": _L1_conv_in["bias"],
        "L1_conv_up_filter": _L1_conv_in["up_filter"],
        "L1_conv_down_filter": _L1_conv_in["down_filter"],
    }

def reference(x, L0_conv_w_down, L0_conv_w_conv, L0_conv_w_up, L1_conv_bias, L1_conv_up_filter, L1_conv_down_filter):
    import jax
    import jax.numpy as jnp
    def _L0_conv_ref(sx, w_down, w_conv, w_up):
        import jax, jax.numpy as jnp
        import numpy as np
        B, CH, H, W = (8, 512, 128, 128)
        K, N = (8, 2)
        KM_ITERS, EM_ITERS = (10, 10)
        EPS = 1e-06

        def _kmeans_labels(xs):
            c = xs.shape[0]
            init_idx = jnp.round(jnp.linspace(0.0, c - 1.0, K)).astype(jnp.int32)
            cent = xs[init_idx]
            x2 = (xs ** 2).sum(1, keepdims=True)
            for _ in range(KM_ITERS):
                d = x2 - 2.0 * (xs @ cent.T) + (cent ** 2).sum(1)[None, :]
                labels = jnp.argmin(d, axis=1)
                oh = jax.nn.one_hot(labels, K, dtype=xs.dtype)
                cnt = oh.sum(0)
                new_cent = oh.T @ xs / jnp.maximum(cnt, 1.0)[:, None]
                cent = jnp.where((cnt > 0.0)[:, None], new_cent, cent)
            d = x2 - 2.0 * (xs @ cent.T) + (cent ** 2).sum(1)[None, :]
            return jnp.argmin(d, axis=1)

        def _gmm_fit(data):
            b, P, k = data.shape
            pick = jnp.round(jnp.linspace(0.0, P - 1.0, N)).astype(jnp.int32)
            mu = data[:, pick, :]
            var = jnp.broadcast_to(data.var(axis=1, keepdims=True) + EPS, mu.shape)
            wts = jnp.full((b, N), 1.0 / N, dtype=data.dtype)
            log2pi = jnp.log(2.0 * jnp.pi).astype(data.dtype)
            for _ in range(EM_ITERS):
                diff2 = ((data[:, :, None, :] - mu[:, None, :, :]) ** 2 / var[:, None, :, :]).sum(-1)
                logdet = jnp.log(var).sum(-1)
                logp = -0.5 * (diff2 + logdet[:, None, :] + k * log2pi) + jnp.log(wts)[:, None, :]
                resp = jax.nn.softmax(logp, axis=2)
                Nk = resp.sum(1)
                mu = jnp.einsum('bpn,bpk->bnk', resp, data) / Nk[..., None]
                ex2 = jnp.einsum('bpn,bpk->bnk', resp, data ** 2) / Nk[..., None]
                var = jnp.maximum(ex2 - mu ** 2 + EPS, EPS)
                wts = Nk / P
            return (mu, var)

        def _bilinear_up_x2(x):
            b, c, h, w = x.shape

            def coords(n_in, n_out):
                s = jnp.linspace(0.0, n_in - 1.0, n_out)
                i0 = jnp.floor(s).astype(jnp.int32)
                i1 = jnp.minimum(i0 + 1, n_in - 1)
                return (i0, i1, (s - i0).astype(x.dtype))
            y0, y1, fy = coords(h, 2 * h)
            x0, x1, fx = coords(w, 2 * w)
            rows = x[:, :, y0, :] * (1.0 - fy)[None, None, :, None] + x[:, :, y1, :] * fy[None, None, :, None]
            return rows[:, :, :, x0] * (1.0 - fx) + rows[:, :, :, x1] * fx

        def _forward(sx, w_down, w_conv, w_up):
            c2 = sx.shape[1] // 2
            x = jax.lax.conv_general_dilated(sx, w_down, window_strides=(2, 2), padding=((1, 1), (1, 1)), feature_group_count=c2, dimension_numbers=('NCHW', 'OIHW', 'NCHW'))
            b, c, h, w = x.shape
            xx = jax.lax.stop_gradient(x[0].reshape(c, h * w))
            mn = xx.min(axis=1, keepdims=True)
            mx = xx.max(axis=1, keepdims=True)
            xs = (xx - mn) / jnp.maximum(mx - mn, 1e-12)
            labels = _kmeans_labels(xs)
            oh = jax.nn.one_hot(labels, K, dtype=xx.dtype)
            cnt = oh.sum(0)
            cl_mean = oh.T @ xx / jnp.maximum(cnt, 1.0)[:, None]
            v22 = cl_mean.std(axis=1)
            order = jnp.argsort(v22)
            inv = jnp.argsort(order)
            slabel = inv[labels]
            soh = jax.nn.one_hot(slabel, K, dtype=x.dtype)
            scnt = soh.sum(0)
            v5 = jnp.einsum('bchw,ck->bkhw', x, soh / jnp.maximum(scnt, 1.0)[None, :])
            wa = jax.lax.stop_gradient(v5.reshape(b, K, h * w).transpose(0, 2, 1))
            mu, var = _gmm_fit(wa)
            v6 = mu.transpose(0, 2, 1)
            v66 = var.transpose(0, 2, 1)
            box = jnp.take_along_axis(v6, jnp.argsort(v66, axis=2), axis=2)
            y = jax.nn.sigmoid(jnp.einsum('bkn,kn->bk', box, w_conv))
            gate = y[:, slabel]
            pre_up = gate[:, :, None, None] * x + x
            up = jnp.repeat(pre_up, 2, axis=1) * w_up[None, :, None, None]
            return _bilinear_up_x2(up) + sx
        return _forward(sx, w_down, w_conv, w_up)

    def _L1_conv_ref(input, bias, up_filter, down_filter):
        import jax, jax.numpy as jnp
        import numpy as np
        UP = 2
        DOWN = 2
        NEG_SLOPE = 0.2
        MARGIN = 10
        FLRELU_SCALE = np.float32(2.0 ** 0.5)
        UP_PAD = ((10 + 1) // 2 + UP - 1, 10 // 2)
        DOWN_PAD = ((10 + 1) // 2, 10 // 2)
        _FILT = np.array([0.0, 0.00398, -0.01884, -0.05155, 0.12443, 0.44197, 0.44197, 0.12443, -0.05155, -0.01884, 0.00398, 0.0], dtype=np.float32)
        _FILT = _FILT / _FILT.sum()

        def _fir1d(x, k, up, down, pad0, pad1, axis):
            N, C, H, W = x.shape
            xr = x.reshape(N * C, 1, H, W)
            K = k.shape[0]
            kf = k[::-1].astype(x.dtype)
            if axis == 3:
                w = kf.reshape(1, 1, 1, K)
                lhs_dil = (1, up)
                strides = (1, down)
                padding = ((0, 0), (pad0, pad1 + up - 1))
            else:
                w = kf.reshape(1, 1, K, 1)
                lhs_dil = (up, 1)
                strides = (down, 1)
                padding = ((pad0, pad1 + up - 1), (0, 0))
            y = jax.lax.conv_general_dilated(xr, w, window_strides=strides, padding=padding, lhs_dilation=lhs_dil, dimension_numbers=('NCHW', 'OIHW', 'NCHW'))
            return y.reshape(N, C, y.shape[2], y.shape[3])

        def _sep_upfirdn(x, k, up, down, pad):
            x = _fir1d(x, k, up, down, pad[0], pad[1], axis=3)
            x = _fir1d(x, k, up, down, pad[0], pad[1], axis=2)
            return x
        out = input + bias[None, :, None, None]
        upf = up_filter * UP
        out = _sep_upfirdn(out, upf, UP, 1, UP_PAD)
        out = jax.nn.leaky_relu(out, NEG_SLOPE) * FLRELU_SCALE
        out = _sep_upfirdn(out, down_filter, 1, DOWN, DOWN_PAD)
        m = (MARGIN * UP - MARGIN * DOWN) // 2
        if m > 0:
            out = out[:, :, m:-m, m:-m]
        return out

    def _gn(v, G=32, eps=1e-5):
        B_, C_, H_, W_ = v.shape
        g = v.reshape(B_, G, C_ // G, H_, W_)
        m = jnp.mean(g, axis=(2, 3, 4), keepdims=True)
        s = jnp.var(g, axis=(2, 3, 4), keepdims=True)
        return ((g - m) / jnp.sqrt(s + eps)).reshape(v.shape)

    def _ln_c(v, eps=1e-6):
        m = jnp.mean(v, axis=1, keepdims=True)
        s = jnp.var(v, axis=1, keepdims=True)
        return (v - m) / jnp.sqrt(s + eps)

    def _ln_t(v, eps=1e-5):
        m = jnp.mean(v, axis=-1, keepdims=True)
        s = jnp.var(v, axis=-1, keepdims=True)
        return (v - m) / jnp.sqrt(s + eps)

    def _to_tokens(v):
        B_, C_, H_, W_ = v.shape
        return v.reshape(B_, C_, H_ * W_).transpose(0, 2, 1)
    def _from_tokens(t, like):
        B_, C_, H_, W_ = like.shape
        return t.transpose(0, 2, 1).reshape(B_, C_, H_, W_)

    x = _L0_conv_ref(x, L0_conv_w_down, L0_conv_w_conv, L0_conv_w_up)
    x = _L1_conv_ref(x, L1_conv_bias, L1_conv_up_filter, L1_conv_down_filter)
    return x


_drawn_inputs = setup_inputs


def setup_inputs(seed=0):
    import zlib

    import numpy as np

    out = dict(_drawn_inputs(seed))
    spreads = {'L1_conv_bias': (0.0, 0.1)}
    factors = {}
    for name, (base, spread) in spreads.items():
        noise = np.random.default_rng([zlib.crc32(name.encode()), seed]).standard_normal(out[name].shape)
        drawn = base * np.exp(spread * noise) if base else spread * noise
        out[name] = jnp.asarray(drawn.astype(out[name].dtype))
    for name, factor in factors.items():
        out[name] = (out[name] * factor).astype(out[name].dtype)
    return out
```

```python
from contextlib import ExitStack

import numpy as np

import concourse.bass as bass
from concourse import mybir

ALU = mybir.AluOpType
ACT = mybir.ActivationFunctionType
AX = mybir.AxisListType
F32 = mybir.dt.float32
F32R = mybir.dt.float32r

P = 128
B, CH, H, W = 8, 512, 128, 128
C = CH // 2
CB = C // P
HO, WO = H // 2, W // 2
PX = HO * WO
TAPS = 2 * 3 * 3
K, N = 8, 2
KM_ITERS, EM_ITERS = 10, 10
EPS = 1e-6
FT = 12
UH, UW = 2 * H, 2 * W
SLOPE, GAIN = 0.2, 2.0 ** 0.5

QR = 16
NQ = HO // QR
IN_ROWS = 2 * QR + 1
V_ROWS = 10
T_ROWS = QR - V_ROWS

GR = P // B
G_PX = PX // GR

UNITS = B * CH // 2
GROUPS = UNITS // 2


def constants():
    p = np.arange(P)
    parts = {}
    parts["ident"] = np.eye(P, dtype=np.float32)
    parts["same_batch"] = (p[:, None] // GR == p[None] // GR).astype(np.float32)
    parts["first_of_batch"] = (p[:, None] == GR * (p[None] // GR)).astype(np.float32)
    parts["last_of_batch"] = (p[:, None] == GR * (p[None] // GR) + GR - 1).astype(np.float32)
    picks = np.round(np.linspace(0.0, C - 1.0, K)).astype(np.int64)
    parts["first_points"] = (p[:, None, None] + P * np.arange(CB)[None, :, None] == picks).astype(np.float32).reshape(P, -1)
    parts["number"] = np.broadcast_to(np.arange(K, dtype=np.float32), (P, K))
    parts["before"] = np.broadcast_to((np.arange(K)[None] < np.arange(K)[:, None]).astype(np.float32), (P, K, K)).reshape(P, -1)
    s = np.linspace(0.0, HO - 1.0, H).astype(np.float32)
    i0 = np.floor(s).astype(np.int64)
    i1 = np.minimum(i0 + 1, HO - 1)
    f = (s - i0).astype(np.float32)
    lin = np.zeros((HO, H), np.float32)
    lin[i0, np.arange(H)] += np.float32(1) - f
    lin[i1, np.arange(H)] += f
    parts["lin"] = np.concatenate([lin, np.zeros((P - HO, H), np.float32)])
    pair = np.zeros((P, 2 * W), np.float32)
    pair[:WO, :W] = lin
    pair[WO:, W:] = lin
    parts["lin_pair"] = pair
    t = np.arange(FT)[None, :, None]
    o = np.arange(UH)[None, None]
    parts["up_taps"] = (o - 2 * p[:, None, None] + 5 == t).astype(np.float32).reshape(P, -1)
    i = p[:, None, None, None] + P * np.arange(2)[None, None, :, None]
    od = np.arange(H)[None, None, None]
    parts["down_taps"] = (6 - i + 2 * od == t[..., None]).astype(np.float32).reshape(P, -1)
    at, n = {}, 0
    for name, a in parts.items():
        at[name] = (n, n + a.shape[1])
        n += a.shape[1]
    return np.ascontiguousarray(np.concatenate(list(parts.values()), axis=1)), at


def build(nc, x, w_down, w_conv, w_up, bias, up_filter, down_filter, consts, out):
    at = constants()[1]
    ctx = ExitStack()
    with ctx:
        def sb(name, shape, dt=F32):
            return ctx.enter_context(nc.sbuf_tensor(name, shape, dt))

        def sem(name):
            return ctx.enter_context(nc.semaphore(name))

        conv_dram = nc.dram_tensor("conv_dram", (B * C, PX), F32, kind="Internal").ap()
        mean_dram = nc.dram_tensor("mean_dram", (B, K, PX), F32, kind="Internal").ap()

        bank = [ctx.enter_context(nc.psum_tensor(f"bank{i}", [P, 512], F32)) for i in range(8)]

        n_small = at["up_taps"][0]
        cst = sb("cst", [P, n_small])
        up_t = sb("up_t", [P, UH])
        down_t = sb("down_t", [P, 2, H])
        up_h = sb("up_h", [P, UH], F32R)
        up_l = sb("up_l", [P, UH], F32R)
        down_h = sb("down_h", [P, 2, H], F32R)
        down_l = sb("down_l", [P, 2, H], F32R)
        up_f = sb("up_f", [P, FT])
        down_f = sb("down_f", [P, FT])
        ones = sb("ones", [P, P])
        w_up_all = sb("w_up_all", [P, CH])
        coef = sb("coef", [P, B * CH])
        bias_all = sb("bias_all", [P, B * CH])
        wc_all = sb("wc_all", [P, K, N])

        def const(name):
            a, b = at[name]
            return cst[:, a:b]

        ident = const("ident")
        number = const("number")

        small_loaded = sem("small_loaded")
        taps_loaded = sem("taps_loaded")
        ready = sem("ready")

        def convolution():
            with ExitStack() as own:
                def sb(name, shape, dt=F32):
                    return own.enter_context(nc.sbuf_tensor(name, shape, dt))

                def sem(name):
                    return own.enter_context(nc.semaphore(name))

                taps = sb("taps", [P, 2 * FT * UH])
                tap_w = sb("tap_w", [P, CB, TAPS])
                diag = sb("diag", [P, CB * TAPS, P])
                rows_in = [sb(f"rows_in{i}", [P, 2, IN_ROWS, W]) for i in range(2)]
                conv = [sb(f"conv{i}", [P, QR, WO]) for i in range(2)]
                in_loaded = [sem(f"in_loaded{i}") for i in range(2)]
                conv_stored = [sem(f"conv_stored{i}") for i in range(2)]
                vec_step = sem("vec_step")
                diag_ready = sem("diag_ready")
                v_done = sem("v_done")
                t_done = sem("t_done")
                t_copied = sem("t_copied")
                UB = CB * NQ
                order = [(i, kh, kw) for i in range(2) for kh in (1, 0, 2) for kw in (1, 0, 2)]

                def conv_in(n, i, kh, kw, r0, r1):
                    c0 = (1, 0, 1)[kw]
                    return rows_in[n % 2][:, i, 2 * r0 + kh:2 * (r1 - 1) + kh + 1:2, c0:c0 + 2 * (63 if kw == 0 else 64) - 1:2]

                block = own.enter_context(nc.Block())

                @block.sync
                def _(sp):
                    sp.dma_start(cst[:], consts[:, 0:n_small]).then_inc(small_loaded, 16)
                    with nc.allow_non_contiguous_dma(reason="a few small weights"):
                        sp.dma_start(tap_w[:], w_down.rearrange("(b c) i h w -> c b (i h w)", b=CB)).then_inc(small_loaded, 16)
                    sp.dma_start(up_f[:], up_filter.rearrange("(o t) -> o t", o=1).to_broadcast([P, FT])).then_inc(small_loaded, 16)
                    sp.dma_start(down_f[:], down_filter.rearrange("(o t) -> o t", o=1).to_broadcast([P, FT])).then_inc(small_loaded, 16)
                    sp.dma_start(w_up_all[:], w_up.rearrange("(o t) -> o t", o=1).to_broadcast([P, CH])).then_inc(small_loaded, 16)
                    sp.dma_start(wc_all[:].rearrange("p k n -> p (k n)"), w_conv.rearrange("k n -> (k n)").rearrange("(o t) -> o t", o=1).to_broadcast([P, K * N])).then_inc(small_loaded, 16)
                    for b in range(B):
                        sp.dma_start(bias_all[:, b * CH:(b + 1) * CH], bias.rearrange("(o t) -> o t", o=1).to_broadcast([P, CH])).then_inc(small_loaded, 16)
                    sp.dma_start(taps[:], consts[:, n_small:n_small + 2 * FT * UH]).then_inc(taps_loaded, 16)

                    def load(b, n, wait):
                        cb, q = n // NQ, n % NQ
                        if wait is not None:
                            sp.wait_ge(v_done, wait)
                            sp.wait_ge(t_done, wait)
                        lo = 1 if q == 0 else 0
                        src = x[bass.ds(b, 1)] if not isinstance(b, int) else x[b:b + 1]
                        src = src.rearrange("o (b c i) h w -> (o b) c i h w", b=CB, i=2)[cb]
                        sp.dma_start(rows_in[n % 2][:, :, lo:, :],
                                     src[:, :, 2 * QR * q - 1 + lo:2 * QR * (q + 1), :]).then_inc(in_loaded[n % 2], 16)

                    for n in range(UB):
                        load(0, n, n - 1 if n >= 2 else None)
                    with sp.Fori(1, B) as b:
                        for n in range(UB):
                            load(b, n, UB * b + n - 1)

                @block.vector
                def _(v):
                    v.memset(ones[:], 1.0).then_inc(ready, 1)
                    v.wait_ge(small_loaded, 16 * (6 + B))
                    v.tensor_tensor(diag[:], ident[:, None, :].to_broadcast([P, CB * TAPS, P]),
                                    tap_w[:].rearrange("p b t -> p (b t)")[:, :, None].to_broadcast([P, CB * TAPS, P]),
                                    ALU.mult).then_inc(diag_ready, 1)
                    v.wait_ge(taps_loaded, 16)
                    v.tensor_scalar(up_f[:], up_f[:], 2.0, None, ALU.mult).then_inc(ready, 1)
                    v.wait_ge(ready, 2)
                    n = 2
                    for t in range(FT):
                        for mat, f, k in ((up_t[:], up_f, 0), (down_t[:].rearrange("p j o -> p (j o)"), down_f, 1)):
                            where = taps[:, (k * FT + t) * UH:(k * FT + t + 1) * UH]
                            if t == 0:
                                v.tensor_scalar(mat, where, f[:, t:t + 1], None, ALU.mult).then_inc(ready, 1)
                            else:
                                v.wait_ge(ready, n - 1)
                                v.scalar_tensor_tensor(out=mat, in0=where, scalar=f[:, t:t + 1], in1=mat,
                                                       op0=ALU.mult, op1=ALU.add).then_inc(ready, 1)
                            n += 1
                    v.wait_ge(ready, n)
                    for full, high in ((up_t, up_h), (down_t, down_h)):
                        v.tensor_copy(high[:], full[:]).then_inc(ready, 1)
                    v.wait_ge(ready, n + 2)
                    for full, high, rest in ((up_t, up_h, up_l), (down_t, down_h, down_l)):
                        v.tensor_tensor(rest[:], full[:], high[:].bitcast(F32), ALU.subtract).then_inc(ready, 1)

                    def unit(b, n, first):
                        cb, q = n // NQ, n % NQ
                        v.wait_ge(in_loaded[n % 2], 16 * (n // 2 + 1) if first else (16 * (UB // 2)) * b + 16 * (n // 2 + 1))
                        if not (first and n < 2):
                            v.wait_ge(conv_stored[n % 2], 16 * (n // 2) if first else (16 * (UB // 2)) * b + 16 * (n // 2))
                        for s, (i, kh, kw) in enumerate(order):
                            r0 = 1 if (q == 0 and kh == 0) else 0
                            dst = conv[n % 2][:, r0:V_ROWS, (1 if kw == 0 else 0):]
                            w = tap_w[:, cb, (i * 3 + kh) * 3 + kw:(i * 3 + kh) * 3 + kw + 1]
                            src = conv_in(n, i, kh, kw, r0, V_ROWS)
                            last = s == TAPS - 1
                            if s == 0:
                                ins = v.tensor_scalar(dst, src, w, None, ALU.mult)
                            else:
                                v.wait_ge(vec_step, (TAPS - 1) * n + s if first else (TAPS - 1) * UB * b + ((TAPS - 1) * n + s))
                                ins = v.scalar_tensor_tensor(out=dst, in0=src, scalar=w, in1=dst, op0=ALU.mult, op1=ALU.add)
                            ins.then_inc(v_done if last else vec_step, 1)

                    for n in range(UB):
                        unit(0, n, True)
                    with v.Fori(1, B) as b:
                        for n in range(UB):
                            unit(b, n, False)

                @block.tensor
                def _(pe):
                    pe.wait_ge(diag_ready, 1)

                    def unit(b, n, first):
                        cb = n // NQ
                        pe.wait_ge(in_loaded[n % 2], 16 * (n // 2 + 1) if first else (16 * (UB // 2)) * b + 16 * (n // 2 + 1))
                        if not (first and n < 2):
                            pe.wait_ge(t_copied, n - 1 if first else UB * b + (n - 1))
                        acc = bank[n % 2][:, 0:T_ROWS * WO].rearrange("p (r w) -> p r w", r=T_ROWS)
                        for s, (i, kh, kw) in enumerate(order):
                            mm = pe.matmul(acc[:, :, (1 if kw == 0 else 0):],
                                           diag[:, cb * TAPS + (i * 3 + kh) * 3 + kw, :],
                                           conv_in(n, i, kh, kw, V_ROWS, QR), start=(s == 0), stop=(s == TAPS - 1),
                                           skip_group_check=True)
                        mm.then_inc(t_done, 1)

                    for n in range(UB):
                        unit(0, n, True)
                    with pe.Fori(1, B) as b:
                        for n in range(UB):
                            unit(b, n, False)

                @block.scalar
                def _(act):
                    def unit(b, n, first):
                        cb, q = n // NQ, n % NQ
                        act.wait_ge(t_done, n + 1 if first else UB * b + (n + 1))
                        if not (first and n < 2):
                            act.wait_ge(conv_stored[n % 2], 16 * (n // 2) if first else (16 * (UB // 2)) * b + 16 * (n // 2))
                        nc.scalar.activation(conv[n % 2][:, V_ROWS:, :].rearrange("p r w -> p (r w)"),
                                             bank[n % 2][:, 0:T_ROWS * WO], ACT.Copy).then_inc(t_copied, 1)
                        act.wait_ge(t_copied, n + 1 if first else UB * b + (n + 1))
                        act.wait_ge(v_done, n + 1 if first else UB * b + (n + 1))
                        rows = conv_dram[cb * P:(cb + 1) * P] if first else conv_dram[bass.ds(C * b + cb * P, P)]
                        act.dma_start(rows[:, q * QR * WO:(q + 1) * QR * WO],
                                      conv[n % 2][:].rearrange("p r w -> p (r w)")).then_inc(conv_stored[n % 2], 16)

                    for n in range(UB):
                        unit(0, n, True)
                    with act.Fori(1, B) as b:
                        for n in range(UB):
                            unit(b, n, False)
                    for i in range(2):
                        act.wait_ge(conv_stored[i], 16 * B * UB // 2)

        def clusters(soh, sohn):
            with ExitStack() as own:
                def sb(name, shape, dt=F32):
                    return own.enter_context(nc.sbuf_tensor(name, shape, dt))

                def sem(name):
                    return own.enter_context(nc.semaphore(name))

                NB = PX // P
                xx = sb("xx", [P, CB, PX])
                xs = sb("xs", [P, CB, PX])
                xs_t = sb("xs_t", [P, NB, C])
                gram = sb("gram", [P, CB, C])
                mn = sb("mn", [P, CB])
                mx = sb("mx", [P, CB])
                rng = sb("rng", [P, CB])
                x2 = sb("x2", [P, CB])
                diag_g = sb("diag_g", [P, CB, P])
                wgt = sb("wgt", [P, CB, K])
                wx = sb("wx", [P, CB, K])
                dist = sb("dist", [P, CB, K])
                best = sb("best", [P, CB])
                far = sb("far", [P, CB, K])
                lab = sb("lab", [P, CB])
                oh = sb("oh", [P, CB, K])
                cnt1 = sb("cnt1", [P, K])
                empty = sb("empty", [P, K])
                ohn = sb("ohn", [P, CB, K])
                cl = sb("cl", [K, PX])
                cl_sum = sb("cl_sum", [K, 1])
                cl_neg = sb("cl_neg", [K, 1])
                spread = sb("spread", [K, 1])
                spread_d = sb("spread_d", [K, K])
                sp_all = sb("sp_all", [P, K])
                less = sb("less", [P, K, K])
                same = sb("same", [P, K, K])
                rank = sb("rank", [P, K])
                slab = sb("slab", [P, CB])
                slab_k = sb("slab_k", [P, CB, K])

                xx_loaded = sem("xx_loaded")
                step = sem("step")
                tr_ready = sem("tr_ready")
                tr_copied = sem("tr_copied")
                xs_ready = sem("xs_ready")
                gram_mm = sem("gram_mm")
                w_ready = sem("w_ready")
                xc_ready = sem("xc_ready")
                wx_ready = sem("wx_ready")
                c2_ready = sem("c2_ready")
                oh_ready = sem("oh_ready")
                cnt_ready = sem("cnt_ready")
                cl_mm = sem("cl_mm")
                cl_copied = sem("cl_copied")
                cl_summed = sem("cl_summed")
                cl_mean = sem("cl_mean")
                cl_spread = sem("cl_spread")
                sd_ready = sem("sd_ready")
                sp_bcast = sem("sp_bcast")
                soh_ready = sem("soh_ready")
                scnt_ready = sem("scnt_ready")
                ITERS = KM_ITERS + 1
                STEPS = 11

                block = own.enter_context(nc.Block())

                @block.sync
                def _(sp):
                    for cb in range(CB):
                        sp.dma_start(xx[:, cb, :], conv_dram[cb * P:(cb + 1) * P]).then_inc(xx_loaded, 16)

                @block.vector
                def _(v):
                    n = 0

                    def chain(ins):
                        nonlocal n
                        n += 1
                        ins.then_inc(step, 1)
                        v.wait_ge(step, n)

                    v.wait_ge(xx_loaded, 16 * CB)
                    v.tensor_reduce(mn[:], xx[:], AX.X, ALU.min).then_inc(step, 1)
                    v.tensor_reduce(mx[:], xx[:], AX.X, ALU.max).then_inc(step, 1)
                    v.wait_ge(step, 2)
                    n = 2
                    chain(v.tensor_tensor(rng[:], mx[:], mn[:], ALU.subtract))
                    chain(v.tensor_scalar(rng[:], rng[:], 1e-12, None, ALU.max))
                    chain(v.reciprocal(rng[:], rng[:]))
                    for cb in range(CB):
                        v.tensor_scalar(xs[:, cb, :], xx[:, cb, :], mn[:, cb:cb + 1], rng[:, cb:cb + 1],
                                        ALU.subtract, ALU.mult).then_inc(xs_ready, 1)
                    v.tensor_copy(wgt[:].rearrange("p b k -> p (b k)"), const("first_points")).then_inc(w_ready, 1)
                    for i in range(CB):
                        v.wait_ge(gram_mm, i + 1)
                        chain(v.tensor_copy(gram[:, i, :], bank[i][:, 0:C]))
                        chain(v.tensor_tensor(diag_g[:, i, :], gram[:, i, i * P:(i + 1) * P], ident, ALU.mult))
                    v.tensor_reduce(x2[:], diag_g[:], AX.X, ALU.add).then_inc(w_ready, 1)
                    v.wait_ge(w_ready, 2)
                    xc = bank[2][:, 0:CB * K].rearrange("p (b k) -> p b k", b=CB)
                    c2 = bank[3][:, 0:K]
                    cnt = bank[4][:, 0:K]
                    base = n

                    with v.Fori(0, ITERS) as r:
                        m = 0

                        def chain_r(ins):
                            nonlocal m
                            m += 1
                            ins.then_inc(step, 1)
                            v.wait_ge(step, r * STEPS + (base + m))

                        v.wait_ge(xc_ready, r + 1)
                        v.tensor_tensor(wx[:], wgt[:], xc, ALU.mult).then_inc(wx_ready, 1)
                        chain_r(v.scalar_tensor_tensor(out=dist[:], in0=xc, scalar=-2.0,
                                                       in1=x2[:, :, None].to_broadcast([P, CB, K]),
                                                       op0=ALU.mult, op1=ALU.add))
                        v.wait_ge(c2_ready, r + 1)
                        chain_r(v.tensor_tensor(dist[:], dist[:], c2[:, None, :].to_broadcast([P, CB, K]), ALU.add))
                        chain_r(v.tensor_reduce(best[:], dist[:], AX.X, ALU.min))
                        chain_r(v.tensor_tensor(far[:], dist[:], best[:, :, None].to_broadcast([P, CB, K]), ALU.is_gt))
                        chain_r(v.scalar_tensor_tensor(out=far[:], in0=far[:], scalar=float(K),
                                                       in1=number[:, None, :].to_broadcast([P, CB, K]),
                                                       op0=ALU.mult, op1=ALU.add))
                        chain_r(v.tensor_reduce(lab[:], far[:], AX.X, ALU.min))
                        v.tensor_tensor(oh[:], number[:, None, :].to_broadcast([P, CB, K]),
                                        lab[:, :, None].to_broadcast([P, CB, K]), ALU.is_equal).then_inc(oh_ready, 1)
                        v.wait_ge(cnt_ready, r + 1)
                        v.tensor_scalar(empty[:], cnt, 0.0, None, ALU.is_equal).then_inc(step, 1)
                        m += 1
                        chain_r(v.tensor_scalar(cnt1[:], cnt, 1.0, None, ALU.max))
                        chain_r(v.reciprocal(cnt1[:], cnt1[:]))
                        v.tensor_tensor(ohn[:], oh[:], cnt1[:, None, :].to_broadcast([P, CB, K]), ALU.mult).then_inc(step, 1)
                        m += 1
                        v.tensor_tensor(wx[:], wgt[:], empty[:, None, :].to_broadcast([P, CB, K]), ALU.mult).then_inc(step, 1)
                        m += 1
                        v.wait_ge(step, r * STEPS + (base + m))
                        v.tensor_tensor(wgt[:], wx[:], ohn[:], ALU.add).then_inc(w_ready, 1)
                        assert m == STEPS, m
                    n = base + ITERS * STEPS

                    v.wait_ge(w_ready, ITERS + 2)
                    v.wait_ge(cl_copied, 8)
                    v.tensor_reduce(cl_sum[:], cl[:], AX.X, ALU.add).then_inc(cl_summed, 1)
                    v.wait_ge(cl_summed, 1)
                    v.tensor_scalar(cl_neg[:], cl_sum[:], -1.0 / PX, None, ALU.mult).then_inc(cl_mean, 1)
                    v.wait_ge(cl_spread, 1)
                    v.tensor_scalar(spread_d[:], ident[0:K, 0:K], spread[:, 0:1], None, ALU.mult).then_inc(sd_ready, 1)
                    v.wait_ge(sp_bcast, 1)
                    chain(v.tensor_copy(sp_all[:], bank[5][:, 0:K]))
                    v_j = sp_all[:, None, :].to_broadcast([P, K, K])
                    v_k = sp_all[:, :, None].to_broadcast([P, K, K])
                    v.tensor_tensor(less[:], v_j, v_k, ALU.is_lt).then_inc(step, 1)
                    n += 1
                    chain(v.tensor_tensor(same[:], v_j, v_k, ALU.is_equal))
                    chain(v.tensor_tensor(same[:], same[:], const("before").rearrange("p (k j) -> p k j", k=K), ALU.mult))
                    chain(v.tensor_tensor(less[:], less[:], same[:], ALU.add))
                    chain(v.tensor_reduce(rank[:], less[:], AX.X, ALU.add))
                    chain(v.tensor_tensor(slab_k[:], oh[:], rank[:, None, :].to_broadcast([P, CB, K]), ALU.mult))
                    chain(v.tensor_reduce(slab[:], slab_k[:], AX.X, ALU.add))
                    v.tensor_tensor(soh[:], number[:, None, :].to_broadcast([P, CB, K]),
                                    slab[:, :, None].to_broadcast([P, CB, K]), ALU.is_equal).then_inc(soh_ready, 1)
                    v.wait_ge(scnt_ready, 1)
                    chain(v.tensor_scalar(cnt1[:], bank[6][:, 0:K], 1.0, None, ALU.max))
                    chain(v.reciprocal(cnt1[:], cnt1[:]))
                    v.tensor_tensor(sohn[:], soh[:], cnt1[:, None, :].to_broadcast([P, CB, K]), ALU.mult).then_inc(soh_ready, 1)
                    v.wait_ge(soh_ready, 2)

                @block.tensor
                def _(pe):
                    for t in range(NB * CB // 4):
                        cb, b0 = t % CB, 4 * (t // CB)
                        pe.wait_ge(xs_ready, cb + 1)
                        if t >= 4:
                            pe.wait_ge(tr_copied, t - 3)
                        for j in range(4):
                            mm = pe.transpose(bank[4 + t % 4][:, j * P:(j + 1) * P], xs[:, cb, (b0 + j) * P:(b0 + j + 1) * P], ident)
                        mm.then_inc(tr_ready, 1)
                    pe.wait_ge(tr_copied, NB * CB // 4)
                    for i in range(CB):
                        for t in range(NB):
                            mm = pe.matmul(bank[i][:, 0:C], xs_t[:, t, i * P:(i + 1) * P], xs_t[:, t, :],
                                           start=(t == 0), stop=(t == NB - 1))
                        mm.then_inc(gram_mm, 1)
                    pe.wait_ge(ready, 1)
                    with pe.Fori(0, ITERS) as r:
                        pe.wait_ge(w_ready, r + 2)
                        for i in range(CB):
                            for j in range(CB):
                                mm = pe.matmul(bank[2][:, i * K:(i + 1) * K], gram[:, j, i * P:(i + 1) * P], wgt[:, j, :],
                                               start=(j == 0), stop=(j == CB - 1))
                        mm.then_inc(xc_ready, 1)
                        pe.wait_ge(wx_ready, r + 1)
                        for j in range(CB):
                            mm = pe.matmul(bank[3][:, 0:K], ones[:], wx[:, j, :], start=(j == 0), stop=(j == CB - 1))
                        mm.then_inc(c2_ready, 1)
                        pe.wait_ge(oh_ready, r + 1)
                        for j in range(CB):
                            mm = pe.matmul(bank[4][:, 0:K], ones[:], oh[:, j, :], start=(j == 0), stop=(j == CB - 1))
                        mm.then_inc(cnt_ready, 1)
                    pe.wait_ge(w_ready, ITERS + 2)
                    for t in range(8):
                        if t >= 2:
                            pe.wait_ge(cl_copied, t - 1)
                        for j in range(CB):
                            mm = pe.matmul(bank[t % 2][0:K, :], ohn[:, j, :], xx[:, j, t * 512:(t + 1) * 512],
                                           start=(j == 0), stop=(j == CB - 1))
                        mm.then_inc(cl_mm, 1)
                    pe.wait_ge(sd_ready, 1)
                    pe.matmul(bank[5][:, 0:K], ones[0:K, :], spread_d[:], start=True, stop=True).then_inc(sp_bcast, 1)
                    pe.wait_ge(soh_ready, 1)
                    for j in range(CB):
                        mm = pe.matmul(bank[6][:, 0:K], ones[:], soh[:, j, :], start=(j == 0), stop=(j == CB - 1))
                    mm.then_inc(scnt_ready, 1)

                @block.scalar
                def _(act):
                    for t in range(NB * CB // 4):
                        cb, b0 = t % CB, 4 * (t // CB)
                        act.wait_ge(tr_ready, t + 1)
                        nc.scalar.activation(xs_t[:, b0:b0 + 4, cb * P:(cb + 1) * P],
                                             bank[4 + t % 4][:].rearrange("p (t c) -> p t c", t=4), ACT.Copy).then_inc(tr_copied, 1)
                    for t in range(8):
                        act.wait_ge(cl_mm, t + 1)
                        nc.scalar.activation(cl[:, t * 512:(t + 1) * 512], bank[t % 2][0:K, :], ACT.Copy).then_inc(cl_copied, 1)
                    act.wait_ge(cl_mean, 1)
                    nc.scalar.activation(xs[0:K, 0, :], cl[:], ACT.Square, bias=cl_neg[:, 0:1],
                                         accum_out=spread[:, 0:1]).then_inc(cl_spread, 1)

        def cluster_means(sohn):
            with ExitStack() as own:
                def sb(name, shape, dt=F32):
                    return own.enter_context(nc.sbuf_tensor(name, shape, dt))

                def sem(name):
                    return own.enter_context(nc.semaphore(name))

                xb = [sb(f"xb{i}", [P, CB, PX]) for i in range(2)]
                cm = [sb(f"cm{i}", [K, PX]) for i in range(2)]
                xb_loaded = [sem(f"xb_loaded{i}") for i in range(2)]
                cm_stored = [sem(f"cm_stored{i}") for i in range(2)]
                cm_mm = sem("cm_mm")
                cm_copied = sem("cm_copied")
                T = PX // 512
                block = own.enter_context(nc.Block())

                @block.sync
                def _(sp):
                    for b in range(B):
                        if b >= 2:
                            sp.wait_ge(cm_mm, T * (b - 1))
                        sp.dma_start(xb[b % 2][:], conv_dram[b * C:(b + 1) * C].rearrange("(j c) p -> c j p", j=CB)).then_inc(xb_loaded[b % 2], 16)

                @block.tensor
                def _(pe):
                    for b in range(B):
                        pe.wait_ge(xb_loaded[b % 2], 16 * (b // 2 + 1))
                        for t in range(T):
                            u = b * T + t
                            if u >= 4:
                                pe.wait_ge(cm_copied, u - 3)
                            for j in range(CB):
                                mm = pe.matmul(bank[u % 4][0:K, :], sohn[:, j, :], xb[b % 2][:, j, t * 512:(t + 1) * 512],
                                               start=(j == 0), stop=(j == CB - 1))
                            mm.then_inc(cm_mm, 1)

                @block.scalar
                def _(act):
                    for b in range(B):
                        if b >= 2:
                            act.wait_ge(cm_stored[b % 2], 16 * (b // 2))
                        for t in range(T):
                            u = b * T + t
                            act.wait_ge(cm_mm, u + 1)
                            nc.scalar.activation(cm[b % 2][:, t * 512:(t + 1) * 512], bank[u % 4][0:K, :], ACT.Copy).then_inc(cm_copied, 1)
                        act.wait_ge(cm_copied, T * (b + 1))
                        act.dma_start(mean_dram[b], cm[b % 2][:]).then_inc(cm_stored[b % 2], 16)
                    for i in range(2):
                        act.wait_ge(cm_stored[i], 16 * B // 2)

        def mixture(soh):
            with ExitStack() as own:
                def sb(name, shape, dt=F32):
                    return own.enter_context(nc.sbuf_tensor(name, shape, dt))

                def sem(name):
                    return own.enter_context(nc.semaphore(name))

                NK = N * K
                data = sb("data", [P, K, G_PX])
                data2 = sb("data2", [P, K, G_PX])
                sq = sb("sq", [P, NK, G_PX])
                maha = sb("maha", [P, N, G_PX])
                top = sb("top", [P, G_PX])
                resp = sb("resp", [P, N, G_PX])
                scrap = sb("scrap", [P, NK, G_PX])
                sums = sb("sums", [P, 2 * NK + N])
                tot = sb("tot", [P, 2 * NK + N])
                inv_nk = sb("inv_nk", [P, N])
                mu = sb("mu", [P, NK])
                mu_neg = sb("mu_neg", [P, NK])
                mu2 = sb("mu2", [P, NK])
                var = sb("var", [P, NK])
                ivar = sb("ivar", [P, NK])
                wts = sb("wts", [P, N])
                lvar = sb("lvar", [P, NK])
                lwts = sb("lwts", [P, N])
                off = sb("off", [P, N])
                swap = sb("swap", [P, K])
                swd = sb("swd", [P, K])
                box = sb("box", [P, N, K])
                z = sb("z", [P, K])
                y = sb("y", [P, K])
                y_t = sb("y_t", [K, P])
                y_b = sb("y_b", [K, B, P])
                soh_t = sb("soh_t", [K, C])

                data_loaded = sem("data_loaded")
                step = sem("em_step")
                moments = sem("moments")
                moments_mm = sem("moments_mm")
                centred = sem("centred")
                squared = sem("squared")
                sq_used = sem("sq_used")
                params = sem("params")
                logs = sem("logs")
                shifted = sem("shifted")
                expd = sem("expd")
                partial = sem("partial")
                total = sem("total")
                z_ready = sem("z_ready")
                e_ready = sem("e_ready")
                y_ready = sem("y_ready")
                yt_mm = sem("yt_mm")
                yb_ready = sem("yb_ready")
                gate_mm = sem("gate_mm")
                gate_used = sem("gate_used")
                block = own.enter_context(nc.Block())

                @block.sync
                def _(sp):
                    for b in range(B):
                        sp.dma_start(data[b * GR:(b + 1) * GR], mean_dram[b].rearrange("k (g p) -> g k p", g=GR)).then_inc(data_loaded, 16)

                @block.vector
                def _(v):
                    n = 0

                    def chain(ins, wait=True):
                        nonlocal n
                        n += 1
                        ins.then_inc(step, 1)
                        if wait:
                            v.wait_ge(step, n)

                    v.wait_ge(data_loaded, 16 * B)
                    chain(v.tensor_tensor(data2[:], data[:], data[:], ALU.mult), False)
                    v.tensor_reduce(sums[:, 0:K], data[:], AX.X, ALU.add).then_inc(moments, 1)
                    v.wait_ge(moments_mm, 1)
                    chain(v.tensor_copy(mu[:], bank[0][:, 0:NK]), False)
                    chain(v.tensor_scalar(mu2[:, 0:K], bank[1][:, 0:K], 1.0 / PX, None, ALU.mult))
                    chain(v.tensor_tensor(scrap[:, 0:K, :], data[:], mu2[:, 0:K, None].to_broadcast([P, K, G_PX]), ALU.subtract))
                    chain(v.tensor_tensor(scrap[:, 0:K, :], scrap[:, 0:K, :], scrap[:, 0:K, :], ALU.mult))
                    v.tensor_reduce(sums[:, K:2 * K], scrap[:, 0:K, :], AX.X, ALU.add).then_inc(moments, 1)
                    v.wait_ge(moments_mm, 2)
                    for i in range(N):
                        chain(v.tensor_scalar(var[:, i * K:(i + 1) * K], bank[2][:, 0:K], 1.0 / PX, EPS, ALU.mult, ALU.add), False)
                    chain(v.memset(wts[:], 1.0 / N), False)
                    v.wait_ge(step, n)
                    v.tensor_scalar(mu_neg[:], mu[:], -1.0, None, ALU.mult).then_inc(params, 1)
                    base = n

                    PER = 1 + (NK - N) + 3 + N + 4 + 8
                    with v.Fori(0, EM_ITERS) as r:
                        m = 0

                        def chain_r(ins, wait=True):
                            nonlocal m
                            m += 1
                            ins.then_inc(step, 1)
                            if wait:
                                v.wait_ge(step, r * PER + (base + m))

                        chain_r(v.reciprocal(ivar[:], var[:]))
                        for k in range(K):
                            for i in range(N):
                                v.wait_ge(squared, r * NK + (k * N + i + 1))
                                src = sq[:, i * K + k, :]
                                s = ivar[:, i * K + k:i * K + k + 1]
                                if k == 0:
                                    v.tensor_scalar(maha[:, i, :], src, s, None, ALU.mult).then_inc(sq_used, 1)
                                else:
                                    v.wait_ge(sq_used if k == 1 else step, r * N + (i + 1) if k == 1 else r * PER + (base + 1 + (k - 2) * N + i + 1))
                                    chain_r(v.scalar_tensor_tensor(out=maha[:, i, :], in0=src, scalar=s, in1=maha[:, i, :],
                                                                   op0=ALU.mult, op1=ALU.add), False)
                        v.wait_ge(logs, 2 * r + 2)
                        chain_r(v.tensor_reduce(off[:], lvar[:].rearrange("p (n k) -> p n k", n=N), AX.X, ALU.add))
                        chain_r(v.tensor_scalar(off[:], off[:], float(K * np.log(2 * np.pi)), -0.5, ALU.add, ALU.mult))
                        chain_r(v.tensor_tensor(off[:], off[:], lwts[:], ALU.add))
                        for i in range(N):
                            chain_r(v.tensor_scalar(maha[:, i, :], maha[:, i, :], -0.5, off[:, i:i + 1], ALU.mult, ALU.add), i == N - 1)
                        chain_r(v.tensor_tensor(top[:], maha[:, 0, :], maha[:, 1, :], ALU.max))
                        v.tensor_tensor(maha[:], maha[:], top[:, None, :].to_broadcast([P, N, G_PX]), ALU.subtract).then_inc(shifted, 1)
                        v.wait_ge(expd, r + 1)
                        chain_r(v.tensor_tensor(top[:], resp[:, 0, :], resp[:, 1, :], ALU.add))
                        chain_r(v.reciprocal(top[:], top[:]))
                        chain_r(v.tensor_tensor(resp[:], resp[:], top[:, None, :].to_broadcast([P, N, G_PX]), ALU.mult))
                        for i in range(N):
                            for src, o in ((data, 0), (data2, NK)):
                                for k in range(K):
                                    v.tensor_tensor_reduce(out=scrap[:, k + K * (i if o == 0 else 1 - i), :],
                                                           in0=src[:, k, :], in1=resp[:, i, :], scale=1.0, scalar=0.0,
                                                           op0=ALU.mult, op1=ALU.add, accum_out=sums[:, o + i * K + k:o + i * K + k + 1]).then_inc(partial, 1)
                                v.wait_ge(partial, r * (4 * K + 1) + (2 * i + (o > 0) + 1) * K)
                        v.tensor_reduce(sums[:, 2 * NK:], resp[:], AX.X, ALU.add).then_inc(partial, 1)
                        v.wait_ge(total, r + 1)
                        chain_r(v.tensor_copy(tot[:], bank[3][:, 0:2 * NK + N]))
                        chain_r(v.reciprocal(inv_nk[:], tot[:, 2 * NK:]))
                        nk = inv_nk[:, :, None].to_broadcast([P, N, K])
                        chain_r(v.tensor_tensor(mu[:].rearrange("p (n k) -> p n k", n=N), tot[:, 0:NK].rearrange("p (n k) -> p n k", n=N), nk, ALU.mult), False)
                        chain_r(v.tensor_tensor(var[:].rearrange("p (n k) -> p n k", n=N), tot[:, NK:2 * NK].rearrange("p (n k) -> p n k", n=N), nk, ALU.mult))
                        chain_r(v.tensor_tensor(mu2[:], mu[:], mu[:], ALU.mult))
                        chain_r(v.tensor_tensor(var[:], var[:], mu2[:], ALU.subtract))
                        chain_r(v.tensor_scalar(var[:], var[:], EPS, EPS, ALU.add, ALU.max), False)
                        chain_r(v.tensor_scalar(wts[:], tot[:, 2 * NK:], 1.0 / PX, None, ALU.mult))
                        v.tensor_scalar(mu_neg[:], mu[:], -1.0, None, ALU.mult).then_inc(params, 1)
                        assert m == PER, (m, PER)
                    n = base + EM_ITERS * PER
                    v.wait_ge(params, EM_ITERS + 1)

                    chain(v.tensor_tensor(swap[:], var[:, 0:K], var[:, K:NK], ALU.is_gt), False)
                    chain(v.tensor_tensor(swd[:], mu[:, K:NK], mu[:, 0:K], ALU.subtract))
                    chain(v.tensor_copy(box[:, 0, :], mu[:, 0:K]), False)
                    chain(v.tensor_copy(box[:, 1, :], mu[:, K:NK]))
                    swi = swap[:].bitcast(mybir.dt.uint32)
                    chain(v.copy_predicated(box[:, 0, :], swi, mu[:, K:NK]), False)
                    chain(v.copy_predicated(box[:, 1, :], swi, mu[:, 0:K]))
                    chain(v.tensor_tensor(box[:], box[:], wc_all[:].rearrange("p k n -> p n k"), ALU.mult))
                    v.tensor_tensor(z[:], box[:, 0, :], box[:, 1, :], ALU.add).then_inc(z_ready, 1)
                    v.wait_ge(e_ready, 1)
                    chain(v.tensor_scalar(y[:], y[:], 1.0, None, ALU.add))
                    v.reciprocal(y[:], y[:]).then_inc(y_ready, 1)
                    v.wait_ge(yt_mm, 1)
                    chain(v.tensor_copy(y_t[:], bank[4][0:K, 0:P]), False)
                    chain(v.tensor_copy(soh_t[:], bank[5][0:K, 0:C]))
                    v.tensor_copy(y_b[:], y_t[:, 0:P:GR][:, :, None].to_broadcast([K, B, P])).then_inc(yb_ready, 1)
                    for b in range(B):
                        v.wait_ge(gate_mm, b + 1)
                        v.scalar_tensor_tensor(out=coef[:, b * CH:(b + 1) * CH].rearrange("p (c i) -> p c i", i=2),
                                               in0=bank[b % 2][:, 0:C, None].to_broadcast([P, C, 2]), scalar=1.0,
                                               in1=w_up_all[:].rearrange("p (c i) -> p c i", i=2),
                                               op0=ALU.add, op1=ALU.mult).then_inc(gate_used, 1)
                    v.wait_ge(gate_used, B)

                @block.tensor
                def _(pe):
                    pe.wait_ge(data_loaded, 16 * B)
                    pe.matmul(bank[0][:, 0:K], const("first_of_batch"), data[:, :, 0], start=True, stop=True)
                    pe.matmul(bank[0][:, K:NK], const("last_of_batch"), data[:, :, G_PX - 1], start=True, stop=True)
                    pe.wait_ge(moments, 1)
                    pe.matmul(bank[1][:, 0:K], const("same_batch"), sums[:, 0:K], start=True, stop=True).then_inc(moments_mm, 1)
                    pe.wait_ge(moments, 2)
                    pe.matmul(bank[2][:, 0:K], const("same_batch"), sums[:, K:2 * K], start=True, stop=True).then_inc(moments_mm, 1)
                    with pe.Fori(0, EM_ITERS) as r:
                        pe.wait_ge(partial, r * (4 * K + 1) + (4 * K + 1))
                        pe.matmul(bank[3][:, 0:2 * NK + N], const("same_batch"), sums[:], start=True, stop=True).then_inc(total, 1)
                    pe.wait_ge(y_ready, 1)
                    pe.transpose(bank[4][0:K, 0:P], y[:], ident)
                    for j in range(CB):
                        mm = pe.transpose(bank[5][0:K, j * P:(j + 1) * P], soh[:, j, :], ident)
                    mm.then_inc(yt_mm, 1)
                    pe.wait_ge(yb_ready, 1)
                    for b in range(B):
                        if b >= 2:
                            pe.wait_ge(gate_used, b - 1)
                        pe.matmul(bank[b % 2][:, 0:C], y_b[:, b, :], soh_t[:], start=True, stop=True).then_inc(gate_mm, 1)

                @block.scalar
                def _(act):
                    with act.Fori(0, EM_ITERS) as r:
                        act.wait_ge(params, r + 1)
                        nc.scalar.activation(lvar[:], var[:], ACT.Ln).then_inc(logs, 1)
                        nc.scalar.activation(lwts[:], wts[:], ACT.Ln).then_inc(logs, 1)
                        for k in range(K):
                            for i in range(N):
                                nc.scalar.activation(sq[:, i * K + k, :], data[:, k, :], ACT.Square,
                                                     bias=mu_neg[:, i * K + k:i * K + k + 1]).then_inc(squared, 1)
                        act.wait_ge(shifted, r + 1)
                        nc.scalar.activation(resp[:], maha[:], ACT.Exp).then_inc(expd, 1)
                    act.wait_ge(z_ready, 1)
                    nc.scalar.activation(y[:], z[:], ACT.Exp, scale=-1.0).then_inc(e_ready, 1)

        def resample():
            with ExitStack() as own:
                def sb(name, shape, dt=F32):
                    return own.enter_context(nc.sbuf_tensor(name, shape, dt))

                def sem(name):
                    return own.enter_context(nc.semaphore(name))

                img = [sb(f"img{i}", [P, 4, W]) for i in range(2)]
                low = [sb(f"low{i}", [HO, 2, WO]) for i in range(2)]
                low_v = [sb(f"low_v{i}", [P, H]) for i in range(2)]
                x_sum = [sb(f"x_sum{i}", [P, 2, W]) for i in range(2)]
                x_h = [sb(f"x_h{i}", [P, 2, W], F32R) for i in range(2)]
                x_l = [sb(f"x_l{i}", [P, 2, W], F32R) for i in range(2)]
                up1_h = [sb(f"up1_h{i}", [P, 2 * UH], F32R) for i in range(2)]
                up1_l = [sb(f"up1_l{i}", [P, 2 * UH], F32R) for i in range(2)]
                act_t = [sb(f"act_t{i}", [P, 2, UH]) for i in range(2)]
                act_l = [[sb(f"act_l{i}_{j}", [P, 2, UH]) for j in range(2)] for i in range(2)]
                dn1_h = [sb(f"dn1_h{i}", [P, 2, 2 * W], F32R) for i in range(2)]
                dn1_l = [sb(f"dn1_l{i}", [P, 2, 2 * W], F32R) for i in range(2)]
                res = [sb(f"res{i}", [P, 4, W]) for i in range(2)]

                img_loaded = [sem(f"img_loaded{i}") for i in range(2)]
                low_loaded = [sem(f"low_loaded{i}") for i in range(2)]
                res_stored = [sem(f"res_stored{i}") for i in range(2)]
                biased = sem("biased")
                b1_mm = sem("b1_mm")
                b1_out = sem("b1_out")
                b2_mm = sem("b2_mm")
                x_summed = sem("x_summed")
                x_high = sem("x_high")
                x_ready = sem("x_ready")
                u1_mm = sem("u1_mm")
                u1_high = sem("u1_high")
                u1_out = sem("u1_out")
                u2_mm = sem("u2_mm")
                slope_out = sem("slope_out")
                leaky_out = sem("leaky_out")
                d1_mm = sem("d1_mm")
                d1_high = sem("d1_high")
                d1_out = sem("d1_out")
                d2_mm = sem("d2_mm")
                res_ready = sem("res_ready")

                images = x.rearrange("b c h w -> h (b c) w")
                results = out.rearrange("b c h w -> h (b c) w")
                lows = conv_dram.rearrange("c (h w) -> h c w", h=HO)
                FIRST, LAST = -2, UNITS + 2
                LOOP0, LOOP1 = 8, UNITS - 4

                def schedule(eng, slot):
                    for u in range(FIRST, LOOP0):
                        slot(u, 0, u)
                    with eng.Fori(LOOP0 // 4, LOOP1 // 4) as r:
                        for m in range(4):
                            slot(None, r, m)
                    for u in range(LOOP1, LAST + 1):
                        slot(u, 0, u)

                def has(u, lag):
                    return u is None or 0 <= u - lag < UNITS

                def cnt(u, r, m, k, per=1, of=1):
                    if u is not None:
                        return (u + k) // of * per
                    return r * (4 // of * per) + (m + k) // of * per

                block = own.enter_context(nc.Block())

                @block.sync
                def _(sp):
                    def slot(u, r, m):
                        if m % 2 or not has(u, -4):
                            return
                        p = (m // 2) % 2
                        g4 = cnt(u, r, m, 4, per=4, of=2)
                        g2 = cnt(u, r, m, 4, per=2, of=2)
                        used = cnt(u, r, m, 2)
                        if u is None:
                            g4, g2, used = sp.snap(g4), sp.snap(g2), sp.snap(used)
                        if not (u is not None and u < 0):
                            sp.wait_ge(x_summed, used)
                        sp.dma_start(img[p][:], images[:, bass.ds(g4, 4), :] if u is None else images[:, g4:g4 + 4, :]).then_inc(img_loaded[p], 16)
                        sp.dma_start(low[p][:], lows[:, bass.ds(g2, 2), :] if u is None else lows[:, g2:g2 + 2, :]).then_inc(low_loaded[p], 16)

                    slot(-4, 0, -4)
                    schedule(sp, slot)

                @block.gpsimd
                def _(pool):
                    def slot(u, r, m):
                        if m % 2 or not has(u, -2):
                            return
                        p = ((m + 2) // 2) % 2
                        pool.wait_ge(img_loaded[p], cnt(u, r, m, 2 + 4, per=16, of=4))
                        g4 = cnt(u, r, m, 2, per=4, of=2)
                        bg = bias_all[:, bass.ds(g4, 4)] if u is None else bias_all[:, g4:g4 + 4]
                        nc.gpsimd.tensor_tensor(img[p][:], img[p][:], bg[:, :, None].to_broadcast([P, 4, W]), ALU.add).then_inc(biased, 1)

                    schedule(pool, slot)

                @block.tensor
                def _(pe):
                    pe.wait_ge(ready, 2 + 2 * FT + 4)

                    def slot(u, r, m):
                        group = m % 2 == 0 and has(u, -2)
                        p = m % 2
                        if group:
                            q = ((m + 2) // 2) % 2
                            pe.wait_ge(low_loaded[q], cnt(u, r, m, 2 + 4, per=16, of=4))
                            if not (u is not None and u < 0):
                                pe.wait_ge(x_summed, cnt(u, r, m, 2))
                            pe.matmul(bank[0][:, 0:H], low[q][:].rearrange("p c w -> p (c w)"), const("lin")[0:HO],
                                      start=True, stop=True).then_inc(b1_mm, 1)
                        if has(u, 0):
                            pe.wait_ge(x_ready, cnt(u, r, m, 1))
                            if not (u is not None and u < 1):
                                pe.wait_ge(u1_out, cnt(u, r, m, 0))
                            for i in range(2):
                                for k, (a, f) in enumerate(((x_h, up_h), (x_h, up_l), (x_l, up_h))):
                                    mm = pe.matmul(bank[1][:, i * UH:(i + 1) * UH], a[p][:, i, :], f[:], start=(k == 0), stop=(k == 2))
                            mm.then_inc(u1_mm, 1)
                        if has(u, 1):
                            pe.wait_ge(u1_out, cnt(u, r, m, 0))
                            for j in range(2):
                                if not (u is not None and u < 2):
                                    pe.wait_ge(leaky_out, cnt(u, r, m, -1, per=2) + (j - 1))
                                for k, (f, a) in enumerate(((up_h, up1_h), (up_l, up1_h), (up_h, up1_l))):
                                    mm = pe.matmul(bank[2 + j][:], f[:, j * P:(j + 1) * P], a[1 - p][:], start=(k == 0), stop=(k == 2))
                                mm.then_inc(u2_mm, 1)
                        if has(u, 2):
                            pe.wait_ge(leaky_out, cnt(u, r, m, -1, per=2))
                            if not (u is not None and u < 3):
                                pe.wait_ge(d1_out, cnt(u, r, m, -2))
                            for k in range(2):
                                for i in range(2):
                                    for j in range(2):
                                        mm = pe.matmul(bank[4][:, (k * 2 + i) * W:(k * 2 + i + 1) * W],
                                                       act_l[p][j][:, i, k * P:(k + 1) * P], down_t[:, j, :],
                                                       start=(j == 0), stop=(j == 1))
                            mm.then_inc(d1_mm, 1)
                        if has(u, 3):
                            pe.wait_ge(d1_out, cnt(u, r, m, -2))
                            if not (u is not None and u < 4):
                                pe.wait_ge(res_ready, cnt(u, r, m, -3))
                            for k in range(2):
                                for i, (f, a) in enumerate(((down_h, dn1_h), (down_l, dn1_h), (down_h, dn1_l))):
                                    mm = pe.matmul(bank[5][:, 0:2 * W], f[:, k, :], a[1 - p][:, k, :],
                                                   start=(k == 0 and i == 0), stop=(k == 1 and i == 2))
                            mm.then_inc(d2_mm, 1)
                        if group:
                            pe.wait_ge(b1_out, cnt(u, r, m, 4, of=2))
                            pe.matmul(bank[0][:, 0:2 * W], low_v[q][:], const("lin_pair"), start=True, stop=True).then_inc(b2_mm, 1)

                    schedule(pe, slot)

                @block.scalar
                def _(act):
                    def slot(u, r, m):
                        p = m % 2
                        if m % 2 == 0 and has(u, -2):
                            q = ((m + 2) // 2) % 2
                            act.wait_ge(b1_mm, cnt(u, r, m, 4, of=2))
                            nc.scalar.activation(low_v[q][:], bank[0][:, 0:H], ACT.Copy).then_inc(b1_out, 1)
                        if has(u, 0):
                            act.wait_ge(u1_mm, cnt(u, r, m, 1))
                            nc.scalar.activation(up1_h[p][:], bank[1][:], ACT.Copy).then_inc(u1_high, 1)
                        if has(u, 1):
                            for j in range(2):
                                act.wait_ge(u2_mm, cnt(u, r, m, 0, per=2) + (j - 1))
                                if not (u is not None and u < 2):
                                    act.wait_ge(leaky_out, cnt(u, r, m, -1, per=2) + (j - 1))
                                nc.scalar.activation(act_t[j][:].rearrange("p i h -> p (i h)"), bank[2 + j][:], ACT.Copy,
                                                     scale=SLOPE * GAIN).then_inc(slope_out, 1)
                        if has(u, 2):
                            act.wait_ge(d1_mm, cnt(u, r, m, -1))
                            nc.scalar.activation(dn1_h[p][:].rearrange("p k w -> p (k w)"), bank[4][:], ACT.Copy).then_inc(d1_high, 1)
                        if has(u, 3):
                            v = (m - 3) % 4
                            act.wait_ge(d2_mm, cnt(u, r, m, -2))
                            if v % 2 == 0 and not (u is not None and u < 7):
                                act.wait_ge(res_stored[v // 2], cnt(u, r, m, -3, per=16, of=4))
                            nc.scalar.activation(res[v // 2][:, 2 * (v % 2):2 * (v % 2) + 2, :].rearrange("p i w -> p (i w)"),
                                                 bank[5][:, 0:2 * W], ACT.Copy).then_inc(res_ready, 1)
                            if v % 2 == 1:
                                act.wait_ge(res_ready, cnt(u, r, m, -2))
                                g4 = (u - 4) * 2 if u is not None else r * 8 + (m - 4) * 2
                                act.dma_start(results[:, bass.ds(g4, 4), :] if u is None else results[:, g4:g4 + 4, :],
                                              res[v // 2][:]).then_inc(res_stored[v // 2], 16)

                    schedule(act, slot)
                    for i in range(2):
                        act.wait_ge(res_stored[i], 16 * GROUPS // 2)

                @block.vector
                def _(v):
                    def slot(u, r, m):
                        if has(u, -1):
                            n = (m + 1) % 4
                            v.wait_ge(b2_mm, cnt(u, r, m, 3, of=2))
                            v.wait_ge(biased, cnt(u, r, m, 3, of=2))
                            if not (u is not None and u < 1):
                                v.wait_ge(u1_mm, cnt(u, r, m, 0))
                            for i in range(2):
                                c0 = cnt(u, r, m, 1, per=2) + i
                                cf = coef[:, bass.ds(c0, 1)] if u is None else coef[:, c0:c0 + 1]
                                ins = v.scalar_tensor_tensor(out=x_sum[n % 2][:, i, :], in0=bank[0][:, (n % 2) * W:(n % 2 + 1) * W], scalar=cf,
                                                             in1=img[n // 2][:, 2 * (n % 2) + i, :], op0=ALU.mult, op1=ALU.add)
                            ins.then_inc(x_summed, 1)
                        if has(u, 3):
                            v.wait_ge(d1_high, cnt(u, r, m, -2))
                            v.tensor_tensor(dn1_l[1 - m % 2][:].rearrange("p k w -> p (k w)"), bank[4][:],
                                            dn1_h[1 - m % 2][:].rearrange("p k w -> p (k w)").bitcast(F32), ALU.subtract).then_inc(d1_out, 1)
                        if has(u, -1):
                            v.wait_ge(x_summed, cnt(u, r, m, 2))
                            v.tensor_copy(x_h[n % 2][:], x_sum[n % 2][:]).then_inc(x_high, 1)
                        if has(u, 0):
                            v.wait_ge(u1_high, cnt(u, r, m, 1))
                            v.tensor_tensor(up1_l[m % 2][:], bank[1][:], up1_h[m % 2][:].bitcast(F32), ALU.subtract).then_inc(u1_out, 1)
                        if has(u, -1):
                            v.wait_ge(x_high, cnt(u, r, m, 2))
                            v.tensor_tensor(x_l[n % 2][:], x_sum[n % 2][:], x_h[n % 2][:].bitcast(F32), ALU.subtract).then_inc(x_ready, 1)
                        if has(u, 1):
                            for j in range(2):
                                v.wait_ge(slope_out, cnt(u, r, m, 0, per=2) + (j - 1))
                                if not (u is not None and u < 3):
                                    v.wait_ge(d1_mm, cnt(u, r, m, -2))
                                v.scalar_tensor_tensor(out=act_l[1 - m % 2][j][:].rearrange("p i h -> p (i h)"), in0=bank[2 + j][:],
                                                       scalar=GAIN, in1=act_t[j][:].rearrange("p i h -> p (i h)"),
                                                       op0=ALU.mult, op1=ALU.max).then_inc(leaky_out, 1)

                    schedule(v, slot)

        soh = sb("soh", [P, CB, K])
        sohn = sb("sohn", [P, CB, K])
        convolution()
        clusters(soh, sohn)
        cluster_means(sohn)
        mixture(soh)
        resample()


_NAMES = ["x", "L0_conv_w_down", "L0_conv_w_conv", "L0_conv_w_up", "L1_conv_bias", "L1_conv_up_filter", "L1_conv_down_filter"]


def kernel(**inputs):
    import concourse.bacc as _bacc
    from concourse.bass_utils import run_bass_kernel_spmd as _run

    nc = _bacc.Bacc("TRN2", target_bir_lowering=False, num_devices=1)
    arrays, args = {}, []
    for name in _NAMES:
        a = np.ascontiguousarray(inputs[name])
        arrays[f"in_{name}"] = a
        args.append(nc.dram_tensor(f"in_{name}", a.shape, mybir.dt.from_np(a.dtype), kind="ExternalInput").ap())
    a = constants()[0]
    arrays["in_consts"] = a
    args.append(nc.dram_tensor("in_consts", a.shape, F32, kind="ExternalInput").ap())
    out = nc.dram_tensor("out_0", (B, CH, H, W), F32, kind="ExternalOutput").ap()
    build(nc, *args, out)
    r = _run(nc, [arrays], core_ids=[0])
    return r.results[0]["out_0"]
```
